# Optimizing a Trainium2 kernel written in Bass

```python
import numpy as np
import jax
import jax.numpy as jnp

def _softmax(x, axis=-1):
    return jax.nn.softmax(x, axis=axis)

def _gelu(x):
    return jax.nn.gelu(x, approximate=True)

def _silu(x):
    return jax.nn.silu(x)

def _sigmoid(x):
    return jax.nn.sigmoid(x)

def _layernorm(x, axis=-1, eps=1e-05):
    m = jnp.mean(x, axis=axis, keepdims=True)
    v = jnp.var(x, axis=axis, keepdims=True)
    return (x - m) / jnp.sqrt(v + eps)

def _scatter_add(tgt, idx, src, axis=0):
    return tgt.at[idx].add(src)

def _segment_sum(src, seg, n):
    return jax.ops.segment_sum(src, seg, n)
kernel_name = 'mk_dlrm_tower_d1_rec_r8_b4df61'

def setup_inputs(seed: int=0):
    np.random.seed(seed)
    _w = jnp.asarray

    def _rec_inputs():
        import jax
        import jax.numpy as jnp
        _tk = jax.random.key(seed)
        ids = jnp.stack([jax.random.randint(jax.random.fold_in(_tk, 200 + f), (512,), 0, v, jnp.int32) for f, v in enumerate([1000, 125000, 1250, 1250, 12500, 1250, 12500, 12500, 12500, 1250, 1250, 1250, 1000, 1000, 12500, 1250, 12500, 12500, 1250, 1250, 12500, 1250, 1000, 1250, 1250, 1250])], axis=1)
        tbl_0 = 0.05 * jax.random.normal(jax.random.fold_in(_tk, 500 + 0), (1000, 128), jnp.float32)
        tbl_1 = 0.05 * jax.random.normal(jax.random.fold_in(_tk, 500 + 1), (125000, 128), jnp.float32)
        tbl_2 = 0.05 * jax.random.normal(jax.random.fold_in(_tk, 500 + 2), (1250, 128), jnp.float32)
        tbl_3 = 0.05 * jax.random.normal(jax.random.fold_in(_tk, 500 + 3), (1250, 128), jnp.float32)
        tbl_4 = 0.05 * jax.random.normal(jax.random.fold_in(_tk, 500 + 4), (12500, 128), jnp.float32)
        tbl_5 = 0.05 * jax.random.normal(jax.random.fold_in(_tk, 500 + 5), (1250, 128), jnp.float32)
        tbl_6 = 0.05 * jax.random.normal(jax.random.fold_in(_tk, 500 + 6), (12500, 128), jnp.float32)
        tbl_7 = 0.05 * jax.random.normal(jax.random.fold_in(_tk, 500 + 7), (12500, 128), jnp.float32)
        tbl_8 = 0.05 * jax.random.normal(jax.random.fold_in(_tk, 500 + 8), (12500, 128), jnp.float32)
        tbl_9 = 0.05 * jax.random.normal(jax.random.fold_in(_tk, 500 + 9), (1250, 128), jnp.float32)
        tbl_10 = 0.05 * jax.random.normal(jax.random.fold_in(_tk, 500 + 10), (1250, 128), jnp.float32)
        tbl_11 = 0.05 * jax.random.normal(jax.random.fold_in(_tk, 500 + 11), (1250, 128), jnp.float32)
        tbl_12 = 0.05 * jax.random.normal(jax.random.fold_in(_tk, 500 + 12), (1000, 128), jnp.float32)
        tbl_13 = 0.05 * jax.random.normal(jax.random.fold_in(_tk, 500 + 13), (1000, 128), jnp.float32)
        tbl_14 = 0.05 * jax.random.normal(jax.random.fold_in(_tk, 500 + 14), (12500, 128), jnp.float32)
        tbl_15 = 0.05 * jax.random.normal(jax.random.fold_in(_tk, 500 + 15), (1250, 128), jnp.float32)
        tbl_16 = 0.05 * jax.random.normal(jax.random.fold_in(_tk, 500 + 16), (12500, 128), jnp.float32)
        tbl_17 = 0.05 * jax.random.normal(jax.random.fold_in(_tk, 500 + 17), (12500, 128), jnp.float32)
        tbl_18 = 0.05 * jax.random.normal(jax.random.fold_in(_tk, 500 + 18), (1250, 128), jnp.float32)
        tbl_19 = 0.05 * jax.random.normal(jax.random.fold_in(_tk, 500 + 19), (1250, 128), jnp.float32)
        tbl_20 = 0.05 * jax.random.normal(jax.random.fold_in(_tk, 500 + 20), (12500, 128), jnp.float32)
        tbl_21 = 0.05 * jax.random.normal(jax.random.fold_in(_tk, 500 + 21), (1250, 128), jnp.float32)
        tbl_22 = 0.05 * jax.random.normal(jax.random.fold_in(_tk, 500 + 22), (1000, 128), jnp.float32)
        tbl_23 = 0.05 * jax.random.normal(jax.random.fold_in(_tk, 500 + 23), (1250, 128), jnp.float32)
        tbl_24 = 0.05 * jax.random.normal(jax.random.fold_in(_tk, 500 + 24), (1250, 128), jnp.float32)
        tbl_25 = 0.05 * jax.random.normal(jax.random.fold_in(_tk, 500 + 25), (1250, 128), jnp.float32)
        _rk = jax.random.fold_in(_tk, 7)
        r_dense_features = -0.000520686 + 1.00062 * jax.random.normal(jax.random.fold_in(_rk, 101), (512, 128), jnp.float32)
        W_top1 = 0.0405887 * jax.random.normal(jax.random.fold_in(_tk, 801), (607, 512), jnp.float32)
        W_top2 = 0.0441942 * jax.random.normal(jax.random.fold_in(_tk, 802), (512, 256), jnp.float32)
        W_top3 = 0.0625 * jax.random.normal(jax.random.fold_in(_tk, 803), (256, 1), jnp.float32)
        b_top1 = jnp.zeros((512,), jnp.float32)
        b_top2 = jnp.zeros((256,), jnp.float32)
        return (r_dense_features, ids, tbl_0, tbl_1, tbl_2, tbl_3, tbl_4, tbl_5, tbl_6, tbl_7, tbl_8, tbl_9, tbl_10, tbl_11, tbl_12, tbl_13, tbl_14, tbl_15, tbl_16, tbl_17, tbl_18, tbl_19, tbl_20, tbl_21, tbl_22, tbl_23, tbl_24, tbl_25, W_top1, b_top1, W_top2, b_top2, W_top3)
    r_dense_features, ids, tbl_0, tbl_1, tbl_2, tbl_3, tbl_4, tbl_5, tbl_6, tbl_7, tbl_8, tbl_9, tbl_10, tbl_11, tbl_12, tbl_13, tbl_14, tbl_15, tbl_16, tbl_17, tbl_18, tbl_19, tbl_20, tbl_21, tbl_22, tbl_23, tbl_24, tbl_25, W_top1, b_top1, W_top2, b_top2, W_top3 = _rec_inputs()

    def _L0_rec_setup():
        import jax, jax.numpy as jnp
        import numpy as np
        B, F, D = (2048, 26, 128)
        key = jax.random.key(seed)
        k1, k2 = jax.random.split(key)
        dense_features = jax.random.normal(k1, (B, D), dtype=jnp.float32)
        sparse_values = jax.random.normal(k2, (B, F, D), dtype=jnp.float32)
        return {'dense_features': dense_features, 'sparse_values': sparse_values}
    _L0_rec_all = _L0_rec_setup()
    _L0_rec_in = {k: v for k, v in _L0_rec_all.items() if k in ()}
    del _L0_rec_all
    return {'r_dense_features': r_dense_features, 'ids': ids, 'tbl_0': tbl_0, 'tbl_1': tbl_1, 'tbl_2': tbl_2, 'tbl_3': tbl_3, 'tbl_4': tbl_4, 'tbl_5': tbl_5, 'tbl_6': tbl_6, 'tbl_7': tbl_7, 'tbl_8': tbl_8, 'tbl_9': tbl_9, 'tbl_10': tbl_10, 'tbl_11': tbl_11, 'tbl_12': tbl_12, 'tbl_13': tbl_13, 'tbl_14': tbl_14, 'tbl_15': tbl_15, 'tbl_16': tbl_16, 'tbl_17': tbl_17, 'tbl_18': tbl_18, 'tbl_19': tbl_19, 'tbl_20': tbl_20, 'tbl_21': tbl_21, 'tbl_22': tbl_22, 'tbl_23': tbl_23, 'tbl_24': tbl_24, 'tbl_25': tbl_25, 'W_top1': W_top1, 'b_top1': b_top1, 'W_top2': W_top2, 'b_top2': b_top2, 'W_top3': W_top3}

def reference(r_dense_features, ids, tbl_0, tbl_1, tbl_2, tbl_3, tbl_4, tbl_5, tbl_6, tbl_7, tbl_8, tbl_9, tbl_10, tbl_11, tbl_12, tbl_13, tbl_14, tbl_15, tbl_16, tbl_17, tbl_18, tbl_19, tbl_20, tbl_21, tbl_22, tbl_23, tbl_24, tbl_25, W_top1, b_top1, W_top2, b_top2, W_top3):
    import jax
    import jax.numpy as jnp

    def _L0_rec_ref(dense_features, sparse_values):
        import jax, jax.numpy as jnp
        import numpy as np
        B, F, D = (2048, 26, 128)
        sd = jnp.einsum('bfd,bd->bf', sparse_values, dense_features)
        ss = jnp.einsum('bfd,bgd->bfg', sparse_values, sparse_values)
        iu, ju = jnp.triu_indices(F, k=1)
        pairs = ss[:, iu, ju]
        return jnp.concatenate([dense_features, sd, pairs], axis=1)
    e = jnp.stack([tbl_0[ids[:, 0]], tbl_1[ids[:, 1]], tbl_2[ids[:, 2]], tbl_3[ids[:, 3]], tbl_4[ids[:, 4]], tbl_5[ids[:, 5]], tbl_6[ids[:, 6]], tbl_7[ids[:, 7]], tbl_8[ids[:, 8]], tbl_9[ids[:, 9]], tbl_10[ids[:, 10]], tbl_11[ids[:, 11]], tbl_12[ids[:, 12]], tbl_13[ids[:, 13]], tbl_14[ids[:, 14]], tbl_15[ids[:, 15]], tbl_16[ids[:, 16]], tbl_17[ids[:, 17]], tbl_18[ids[:, 18]], tbl_19[ids[:, 19]], tbl_20[ids[:, 20]], tbl_21[ids[:, 21]], tbl_22[ids[:, 22]], tbl_23[ids[:, 23]], tbl_24[ids[:, 24]], tbl_25[ids[:, 25]]], axis=1)
    z = _L0_rec_ref(r_dense_features, e)
    z = z.reshape(z.shape[0], -1)
    h = jnp.concatenate([z, r_dense_features], axis=1)
    h = jnp.maximum(h @ W_top1 + b_top1, 0.0)
    h = jnp.maximum(h @ W_top2 + b_top2, 0.0)
    y = h @ W_top3
    return y

_drawn_inputs = setup_inputs


def setup_inputs(seed=0):
    import zlib

    import numpy as np

    out = dict(_drawn_inputs(seed))
    spreads = {'b_top1': (0.0, 0.1), 'b_top2': (0.0, 0.1)}
    factors = {}
    for name, (base, spread) in spreads.items():
        noise = np.random.default_rng([zlib.crc32(name.encode()), seed]).standard_normal(out[name].shape)
        drawn = base * np.exp(spread * noise) if base else spread * noise
        out[name] = jnp.asarray(drawn.astype(out[name].dtype))
    for name, factor in factors.items():
        out[name] = (out[name] * factor).astype(out[name].dtype)
    return out
```

```python
import concourse.bass as bass
from concourse import mybir
from contextlib import ExitStack


def dlrm_tower(nc, dense_t, ids, ids_t, tables, w1, b1_t, w2, b2_t, w3_t, out):
    fp32 = mybir.dt.float32
    i32 = mybir.dt.int32
    ALU = mybir.AluOpType
    ACT = mybir.ActivationFunctionType

    P = 128
    D, B = dense_t.shape
    F = len(tables)
    N = F + 1
    SLOT = 32
    TILES = B // P
    H1, H2 = w2.shape
    H1B, H2B = H1 // P, H2 // P
    PAIRS = N * (N - 1) // 2
    KC = 3
    KP = PAIRS // KC
    PAIR0 = [g * (N - 1) - g * (g - 1) // 2 for g in range(N)]
    HALF = SLOT // 2

    BY_PRODUCT = [f for f in (0, 12, 13, 22, 23, 24) if tables[f].shape[0] <= 10 * P]
    GATHERED = [f for f in range(F) if f not in BY_PRODUCT]
    GROUP = 4
    GROUPS = [GATHERED[i:i + GROUP] for i in range(0, len(GATHERED), GROUP)]
    NG = len(GROUPS)

    def full(f):
        return tables[f].shape[0] // P

    def chunks(f):
        rows = tables[f].shape[0]
        return [P] * full(f) + ([rows % P] if rows % P else [])

    MAXC = max(len(chunks(f)) for f in BY_PRODUCT)
    SIZES = sorted({tables[f].shape[0] for f in BY_PRODUCT})
    TBUF = 3
    OBUF = 8
    JBUF = 3

    JOBS = []
    flips = [(t, g) for t in range(TILES) for g in range(NG)]
    for n in range(len(BY_PRODUCT)):
        JOBS.append(("product", n, None))
        for _ in range(2):
            JOBS.append(("flip", *flips.pop(0)))
    for t in range(TILES):
        while flips and flips[0][0] <= t:
            JOBS.append(("flip", *flips.pop(0)))
        for stage in ("gram", "turn", "layer1", "layer2", "layer3"):
            JOBS.append((stage, t, None))
    COLUMN_JOBS = [j for j in JOBS if j[0] in ("product", "flip")]

    def column_jobs_for(t):
        return 1 + max(n for n, j in enumerate(COLUMN_JOBS) if j[0] == "product" or j[1] <= t)

    def runs(group):
        found = []
        for i, f in enumerate(group):
            if found and found[-1][1] + found[-1][2] == f:
                found[-1][2] += 1
            else:
                found.append([i, f, 1])
        return found

    with ExitStack() as ctx:
        def sb(name, shape, dt=fp32):
            return ctx.enter_context(nc.sbuf_tensor(name, shape, dt))

        def ps(name, shape):
            return ctx.enter_context(nc.psum_tensor(name, shape, fp32))

        def sem(name):
            return ctx.enter_context(nc.semaphore(name))

        index = sb("index", [P, TILES, F], i32)
        id_row = sb("id_row", [P, len(BY_PRODUCT), B], i32)
        row_of = {s: sb(f"row_of_{s}", [P, MAXC]) for s in SIZES}
        table = sb("table", [P, TBUF, MAXC, D])
        onehot = sb("onehot", [P, OBUF, B])
        rows = sb("rows", [P, TILES, len(GATHERED), D])
        et = sb("et", [P, B, SLOT])
        dense = sb("dense", [P, B])
        ident = sb("ident", [P, P])
        w1d = sb("w1d", [P, 2, H1])
        w1s = sb("w1s", [P, H1])
        w1p = sb("w1p", [KP, KC, H1])
        w2s = sb("w2s", [P, H1B, H2])
        w3s = sb("w3s", [P, H2B])
        b1s = sb("b1s", [P, H1B])
        b2s = sb("b2s", [P, H2B])
        gram_t = sb("gram_t", [P, F, SLOT])
        pairs = sb("pairs", [P, PAIRS])
        pairs_t = sb("pairs_t", [KP, KC, P])
        h1 = sb("h1", [P, H1B, P])
        h2 = sb("h2", [P, H2B, P])
        y = sb("y", [1, B])

        job_ps = ps("job_ps", [P, JBUF, 512])
        gram_ps = ps("gram_ps", [P, 2, 512])
        z_ps = ps("z_ps", [P, 512])
        h1_ps = ps("h1_ps", [P, 2, 512])

        index_loaded = sem("index_loaded")
        id_row_loaded = [sem(f"id_row_loaded_{n}") for n in range(len(BY_PRODUCT))]
        table_loaded = [sem(f"table_loaded_{n}") for n in range(len(BY_PRODUCT))]
        dense_loaded = sem("dense_loaded")
        w1d_loaded = sem("w1d_loaded")
        w1p_loaded = sem("w1p_loaded")
        w2_loaded = sem("w2_loaded")
        small_loaded = sem("small_loaded")
        gathered = [[sem(f"gathered_{t}_{g}") for g in range(NG)] for t in range(TILES)]
        ident_zeroed = sem("ident_zeroed")
        ident_ready = sem("ident_ready")
        row_of_ready = sem("row_of_ready")
        pad_zeroed = sem("pad_zeroed")
        dense_placed = sem("dense_placed")
        w1_summed = sem("w1_summed")
        onehot_ready = sem("onehot_ready")
        onehot_used = sem("onehot_used")
        flip_done = sem("flip_done")
        job_drained = sem("job_drained")
        gram_done = sem("gram_done")
        gram_turned = sem("gram_turned")
        pairs_packed = sem("pairs_packed")
        pairs_turned = sem("pairs_turned")
        pairs_t_ready = sem("pairs_t_ready")
        h1_done = sem("h1_done")
        h1_ready = sem("h1_ready")
        h2_done = sem("h2_done")
        h2_ready = sem("h2_ready")
        y_done = sem("y_done")
        y_ready = sem("y_ready")
        stored = sem("stored")

        def chunks_before(n):
            return sum(len(chunks(f)) for f in BY_PRODUCT[:n])

        block = ctx.enter_context(nc.Block())

        @block.sync
        def _(sp):
            sp.dma_start(index[:], ids.rearrange("(t p) f -> p t f", p=P)).then_inc(index_loaded, 16)
            for n, f in enumerate(BY_PRODUCT):
                sp.dma_start(id_row[:, n, :], ids_t[f:f + 1, :].to_broadcast([P, B])).then_inc(id_row_loaded[n], 16)
                if n >= TBUF:
                    sp.wait_ge(onehot_used, chunks_before(n - TBUF + 1))
                c, rest = full(f), tables[f].shape[0] % P
                sp.dma_start(table[:, n % TBUF, 0:c, :],
                             tables[f][0:c * P, :].rearrange("(p c) d -> p c d", c=c)).then_inc(table_loaded[n], 16)
                if rest:
                    sp.dma_start(table[0:rest, n % TBUF, c, :], tables[f][c * P:c * P + rest, :])\
                      .then_inc(table_loaded[n], 16)
            sp.wait_ge(y_ready, TILES)
            sp.dma_start(out.rearrange("b a -> a b"), y[:]).then_inc(stored, 16)
            sp.wait_ge(stored, 16)

        @block.gpsimd
        def _(pool):
            nc.gpsimd.memset(ident[:], 0.0).then_inc(ident_zeroed, 1)
            for s in SIZES:
                c = s // P
                nc.gpsimd.iota(row_of[s][:, 0:c], [[1, c]], base=0, channel_multiplier=c,
                               allow_small_or_imprecise_dtypes=True).then_inc(row_of_ready, 1)
                nc.gpsimd.iota(row_of[s][:, c:c + 1], [[0, 1]], base=c * P, channel_multiplier=1,
                               allow_small_or_imprecise_dtypes=True).then_inc(row_of_ready, 1)
            pool.wait_ge(ident_zeroed, 1)
            nc.gpsimd.affine_select(out=ident[:], in_=ident[:], compare_op=ALU.not_equal, fill=1.0, base=0,
                                    pattern=[[-1, P]], channel_multiplier=1).then_inc(ident_ready, 1)
            pool.wait_ge(index_loaded, 16)
            for t in range(TILES):
                for g, group in enumerate(GROUPS):
                    for i, f in enumerate(group):
                        nc.gpsimd.indirect_dma_start(
                            rows[:, t, g * GROUP + i, :], None, tables[f],
                            bass.IndirectOffsetOnAxis(index[:, t, f:f + 1], 0)).then_inc(gathered[t][g], 16)

        @block.vector
        def _(dve):
            nc.vector.memset(et[:, :, N:SLOT], 0.0).then_inc(pad_zeroed, 1)
            dve.wait_ge(row_of_ready, 2 * len(SIZES))

            done = [0]

            def make_onehots(n, f):
                dve.wait_ge(id_row_loaded[n], 16)
                for c, k in enumerate(chunks(f)):
                    if done[0] >= OBUF:
                        dve.wait_ge(onehot_used, done[0] - OBUF + 1)
                    nc.vector.tensor_scalar(onehot[0:k, done[0] % OBUF, :], id_row[0:k, n, :],
                                            row_of[tables[f].shape[0]][0:k, c:c + 1], None,
                                            ALU.is_equal).then_inc(onehot_ready, 1)
                    done[0] += 1

            def pack_pairs(t):
                dve.wait_ge(gram_done, t + 1)
                if t:
                    dve.wait_ge(pairs_packed, F * t)
                nc.vector.transpose(
                    gram_t[:].rearrange("p g (k i) -> p g k i", k=2),
                    gram_ps[:, :, 0:HALF * N].rearrange("p k (i g) -> p g k i", g=N)[:, 0:F])\
                    .then_inc(gram_turned, 1)
                dve.wait_ge(gram_turned, t + 1)
                if t:
                    dve.wait_ge(pairs_turned, t)
                for g in range(F):
                    nc.vector.tensor_copy(pairs[:, PAIR0[g]:PAIR0[g] + F - g],
                                          gram_t[:, g, g + 1:N]).then_inc(pairs_packed, 1)

            for kind, a, b in JOBS:
                if kind == "product":
                    make_onehots(a, BY_PRODUCT[a])
                    if a == 0:
                        dve.wait_ge(w1d_loaded, 32)
                        nc.vector.tensor_tensor(w1s[:], w1d[:, 0, :], w1d[:, 1, :], ALU.add).then_inc(w1_summed, 1)
                elif kind == "gram":
                    pack_pairs(a)

        @block.scalar
        def _(act):
            act.dma_start(dense[:], dense_t).then_inc(dense_loaded, 16)
            act.dma_start(w1d[:, 0, :], w1[0:P, :]).then_inc(w1d_loaded, 16)
            act.dma_start(w1d[:, 1, :], w1[P + PAIRS:, :]).then_inc(w1d_loaded, 16)
            act.dma_start(w1p[:], w1[P:P + PAIRS, :].rearrange("(c p) n -> p c n", p=KP)).then_inc(w1p_loaded, 16)
            act.dma_start(w2s[:], w2.rearrange("(c p) n -> p c n", p=P)).then_inc(w2_loaded, 16)
            act.dma_start(b1s[:], b1_t).then_inc(small_loaded, 16)
            act.dma_start(b2s[:], b2_t).then_inc(small_loaded, 16)
            act.dma_start(w3s[:], w3_t).then_inc(small_loaded, 16)
            act.wait_ge(dense_loaded, 16)
            nc.scalar.activation(et[:, :, 0], dense[:], ACT.Copy).then_inc(dense_placed, 1)

            drained = 0
            for kind, a, b in JOBS:
                if kind == "product":
                    act.wait_ge(onehot_used, chunks_before(a + 1))
                    nc.scalar.activation(et[:, :, BY_PRODUCT[a] + 1], job_ps[:, drained % JBUF, :],
                                         ACT.Copy).then_inc(job_drained, 1)
                    drained += 1
                elif kind == "flip":
                    act.wait_ge(flip_done, NG * a + b + 1)
                    found = runs(GROUPS[b])
                    for i, f, k in found:
                        copy = nc.scalar.activation(
                            et[:, a * P:(a + 1) * P, f + 1:f + 1 + k].rearrange("p b f -> p f b"),
                            job_ps[:, drained % JBUF, i * P:(i + k) * P].rearrange("p (f b) -> p f b", b=P),
                            ACT.Copy)
                    copy.then_inc(job_drained, 1)
                    drained += 1
                elif kind == "turn":
                    act.wait_ge(pairs_turned, a + 1)
                    if a:
                        act.wait_ge(h1_done, 2 * a)
                    nc.scalar.activation(pairs_t[:].rearrange("p c b -> p (c b)"), z_ps[0:KP, 0:KC * P],
                                         ACT.Copy).then_inc(pairs_t_ready, 1)
                elif kind == "layer1":
                    if a == 0:
                        act.wait_ge(small_loaded, 48)
                    else:
                        act.wait_ge(h2_done, a)
                    for m in range(H1B):
                        act.wait_ge(h1_done, 2 * a + m // 2 + 1)
                        nc.scalar.activation(h1[:, m, :], h1_ps[:, m // 2, (m % 2) * P:(m % 2 + 1) * P],
                                             ACT.Relu, bias=b1s[:, m:m + 1]).then_inc(h1_ready, 1)
                elif kind == "layer2":
                    act.wait_ge(h2_done, a + 1)
                    if a:
                        act.wait_ge(y_done, a)
                    for m in range(H2B):
                        nc.scalar.activation(h2[:, m, :], z_ps[:, m * P:(m + 1) * P], ACT.Relu,
                                             bias=b2s[:, m:m + 1]).then_inc(h2_ready, 1)
                elif kind == "layer3":
                    act.wait_ge(y_done, a + 1)
                    nc.scalar.activation(y[:, a * P:(a + 1) * P], h1_ps[0:1, 0, 0:P], ACT.Copy)\
                      .then_inc(y_ready, 1)

        @block.tensor
        def _(pe):
            pe.wait_ge(ident_ready, 1)
            jobs = 0
            for kind, a, b in JOBS:
                if kind in ("product", "flip"):
                    bank = jobs % JBUF
                    if jobs >= JBUF:
                        pe.wait_ge(job_drained, jobs - JBUF + 1)
                    jobs += 1
                if kind == "product":
                    rest = tables[BY_PRODUCT[a]].shape[0] % P
                    pe.wait_ge(table_loaded[a], 32 if rest else 16)
                    sizes = chunks(BY_PRODUCT[a])
                    for c, k in enumerate(sizes):
                        used = chunks_before(a) + c
                        pe.wait_ge(onehot_ready, used + 1)
                        nc.tensor.matmul(job_ps[:, bank, :], table[0:k, a % TBUF, c, :],
                                         onehot[0:k, used % OBUF, :], start=c == 0,
                                         stop=c == len(sizes) - 1).then_inc(onehot_used, 1)
                elif kind == "flip":
                    pe.wait_ge(gathered[a][b], 16 * len(GROUPS[b]))
                    for i in range(len(GROUPS[b])):
                        flip = nc.tensor.transpose(job_ps[:, bank, i * P:(i + 1) * P],
                                                   rows[:, a, b * GROUP + i, :], ident[:])
                    flip.then_inc(flip_done, 1)
                elif kind == "gram":
                    pe.wait_ge(job_drained, column_jobs_for(a))
                    if a == 0:
                        pe.wait_ge(dense_placed, 1)
                        pe.wait_ge(pad_zeroed, 1)
                    else:
                        pe.wait_ge(gram_turned, a)
                    for q in range(P // SLOT):
                        for i in range(SLOT):
                            e = et[:, a * P + q * SLOT + i, :]
                            o = (i % HALF) * N
                            gram = nc.tensor.matmul(gram_ps[q * SLOT:(q + 1) * SLOT, i // HALF, o:o + N],
                                                    e, e[:, 0:N], start=True, stop=True)
                    gram.then_inc(gram_done, 1)
                elif kind == "turn":
                    if a:
                        pe.wait_ge(h2_ready, H2B * a)
                    for c in range(KC):
                        pe.wait_ge(pairs_packed, F * a + sum(PAIR0[g] < (c + 1) * KP for g in range(F)))
                        turn = nc.tensor.transpose(z_ps[0:KP, c * P:(c + 1) * P],
                                                   pairs[:, c * KP:(c + 1) * KP], ident[:])
                    turn.then_inc(pairs_turned, 1)
                elif kind == "layer1":
                    if a == 0:
                        pe.wait_ge(w1_summed, 1)
                        pe.wait_ge(dense_loaded, 16)
                        pe.wait_ge(w1p_loaded, 16)
                    else:
                        pe.wait_ge(y_ready, a)
                    for m in range(H1B):
                        o = h1_ps[:, m // 2, (m % 2) * P:(m % 2 + 1) * P]
                        nc.tensor.matmul(o, w1s[:, m * P:(m + 1) * P], dense[:, a * P:(a + 1) * P],
                                         start=True, stop=False)
                        if m == 0:
                            pe.wait_ge(pairs_t_ready, a + 1)
                        for c in range(KC):
                            layer = nc.tensor.matmul(o, w1p[:, c, m * P:(m + 1) * P], pairs_t[:, c, :],
                                                     start=False, stop=c == KC - 1)
                        if m % 2:
                            layer.then_inc(h1_done, 1)
                elif kind == "layer2":
                    if a == 0:
                        pe.wait_ge(w2_loaded, 16)
                    for m in range(H2B):
                        for c in range(H1B):
                            if m == 0:
                                pe.wait_ge(h1_ready, H1B * a + c + 1)
                            layer = nc.tensor.matmul(z_ps[:, m * P:(m + 1) * P], w2s[:, c, m * P:(m + 1) * P],
                                                     h1[:, c, :], start=c == 0, stop=c == H1B - 1)
                    layer.then_inc(h2_done, 1)
                else:
                    pe.wait_ge(h2_ready, H2B * (a + 1))
                    if a == 0:
                        pe.wait_ge(small_loaded, 48)
                    for c in range(H2B):
                        layer = nc.tensor.matmul(h1_ps[0:1, 0, 0:P], w3s[:, c:c + 1], h2[:, c, :],
                                                 start=c == 0, stop=c == H2B - 1)
                    layer.then_inc(y_done, 1)


def kernel(**inputs):
    import numpy as np
    import concourse.bacc as bacc
    from concourse.bass_utils import run_bass_kernel_spmd

    def columns(v):
        return v.reshape(-1, 128).T

    given = {
        "dense_t": np.asarray(inputs["r_dense_features"]).T,
        "ids": np.asarray(inputs["ids"]),
        "ids_t": np.asarray(inputs["ids"]).T,
        **{f"tbl_{f}": np.asarray(inputs[f"tbl_{f}"]) for f in range(26)},
        "w1": np.asarray(inputs["W_top1"]),
        "b1_t": columns(np.asarray(inputs["b_top1"])),
        "w2": np.asarray(inputs["W_top2"]),
        "b2_t": columns(np.asarray(inputs["b_top2"])),
        "w3_t": columns(np.asarray(inputs["W_top3"])),
    }
    nc = bacc.Bacc("TRN2", target_bir_lowering=False, num_devices=1)
    arrays, aps = {}, {}
    for name, array in given.items():
        arrays[name] = np.ascontiguousarray(array)
        aps[name] = nc.dram_tensor(name, arrays[name].shape, mybir.dt.from_np(arrays[name].dtype),
                                   kind="ExternalInput").ap()
    out = nc.dram_tensor("out", (512, 1), mybir.dt.float32, kind="ExternalOutput").ap()
    dlrm_tower(nc, aps["dense_t"], aps["ids"], aps["ids_t"], [aps[f"tbl_{f}"] for f in range(26)],
               aps["w1"], aps["b1_t"], aps["w2"], aps["b2_t"], aps["w3_t"], out)
    return run_bass_kernel_spmd(nc, [arrays], core_ids=[0]).results[0]["out"]
```

```python
import concourse.bass as bass
from concourse import mybir
from contextlib import ExitStack


def dlrm_tower(nc, dense_t, ids, ids_t, tables, w1, b1_t, w2, b2_t, w3_t, out):
    fp32 = mybir.dt.float32
    fp32r = mybir.dt.float32r
    i32 = mybir.dt.int32
    ALU = mybir.AluOpType
    ACT = mybir.ActivationFunctionType

    P = 128
    D, B = dense_t.shape
    F = len(tables)
    N = F + 1
    BLOCK = 32
    SLOT = 28
    TILES = B // P
    H1, H2 = w2.shape
    H1B, H2B = H1 // P, H2 // P
    PAIRS = N * (N - 1) // 2
    KC = 3
    KP = PAIRS // KC
    PAIR0 = [g * (N - 1) - g * (g - 1) // 2 for g in range(N)]
    HALF = BLOCK // 2

    BY_PRODUCT = [f for f in (0, 12, 13, 22, 23, 24, 25, 11, 10) if tables[f].shape[0] <= 10 * P]
    GATHERED = [f for f in range(F) if f not in BY_PRODUCT]
    GROUP = 4
    GROUPS = [GATHERED[i:i + GROUP] for i in range(0, len(GATHERED), GROUP)]
    NG = len(GROUPS)

    def full(f):
        return tables[f].shape[0] // P

    def chunks(f):
        rows = tables[f].shape[0]
        return [P] * full(f) + ([rows % P] if rows % P else [])

    MAXC = max(len(chunks(f)) for f in BY_PRODUCT)
    SIZES = sorted({tables[f].shape[0] for f in BY_PRODUCT})
    TBUF = 2
    IBUF = 4
    OBUF = 8
    JBUF = 2
    GBUF = 2

    JOBS = []
    flips = [("flip", t, g) for t in range(TILES) for g in range(NG)]
    for n in range(len(BY_PRODUCT)):
        JOBS.append(("product", n, None))
        if n > 0:
            JOBS += [flips.pop(0)]
            if n % 4 == 3:
                JOBS += [flips.pop(0)]
    while flips[0][1] == 0:
        JOBS.append(flips.pop(0))
    GQ = BLOCK
    grams = [[("gram", t, q) for q in range(P // GQ)] for t in range(TILES)]
    JOBS += grams[0]
    for t in range(TILES):
        flip = [flips.pop(0) for _ in range(len(flips)) if flips[0][1] == t + 1]
        JOBS += flip
        if t + 1 < TILES:
            JOBS += grams[t + 1][:-1]
        JOBS.append(("turn", t, None))
        if t + 1 < TILES:
            JOBS += grams[t + 1][-1:]
        JOBS.append(("layer1", t, None))
        JOBS += flips[:1]
        JOBS.append(("layer2", t, None))
        JOBS += flips[1:2]
        JOBS.append(("layer3", t, None))
        flips = flips[2:]
    COLUMN_JOBS = [j for j in JOBS if j[0] in ("product", "flip")]

    def column_jobs_for(t):
        return 1 + max(n for n, j in enumerate(COLUMN_JOBS) if j[0] == "product" or j[1] <= t)

    def runs(group):
        found = []
        for i, f in enumerate(group):
            if found and found[-1][1] + found[-1][2] == f:
                found[-1][2] += 1
            else:
                found.append([i, f, 1])
        return found

    with ExitStack() as ctx:
        def sb(name, shape, dt=fp32):
            return ctx.enter_context(nc.sbuf_tensor(name, shape, dt))

        def ps(name, shape):
            return ctx.enter_context(nc.psum_tensor(name, shape, fp32))

        def sem(name):
            return ctx.enter_context(nc.semaphore(name))

        index = sb("index", [P, TILES, F], i32)
        id_row = sb("id_row", [P, IBUF, B], i32)
        row_of = {s: sb(f"row_of_{s}", [P, MAXC]) for s in SIZES}
        table = sb("table", [P, TBUF, MAXC, D])
        table_hi = sb("table_hi", [P, TBUF, MAXC, D], fp32r)
        table_lo = sb("table_lo", [P, TBUF, MAXC, D], fp32r)
        onehot = sb("onehot", [P, OBUF, B], fp32r)
        rows = sb("rows", [P, TILES, len(GATHERED), D])
        et = sb("et", [P, B, SLOT])
        dense = sb("dense", [P, B])
        ident = sb("ident", [P, P])
        w1d = sb("w1d", [P, 2, H1])
        w1s = sb("w1s", [P, H1])
        w1p = sb("w1p", [KP, KC, H1])
        w2s = sb("w2s", [P, H1B, H2])
        w3s = sb("w3s", [P, H2B])
        b1s = sb("b1s", [P, H1B])
        b2s = sb("b2s", [P, H2B])
        gram_t = sb("gram_t", [P, F, BLOCK])
        pairs = sb("pairs", [P, PAIRS])
        pairs_t = sb("pairs_t", [KP, KC, P])
        h1 = sb("h1", [P, H1B, P])
        h2 = sb("h2", [P, H2B, P])
        y = sb("y", [1, B])

        job_ps = ps("job_ps", [P, JBUF, 512])
        gram_ps = ps("gram_ps", [P, GBUF, 2, 512])
        z_ps = ps("z_ps", [P, 512])
        h_ps = ps("h_ps", [P, 512])

        index_loaded = sem("index_loaded")
        id_row_loaded = [sem(f"id_row_loaded_{n}") for n in range(len(BY_PRODUCT))]
        table_loaded = [sem(f"table_loaded_{n}") for n in range(len(BY_PRODUCT))]
        dense_loaded = sem("dense_loaded")
        w1d_loaded = sem("w1d_loaded")
        w1p_loaded = sem("w1p_loaded")
        w2_loaded = sem("w2_loaded")
        small_loaded = sem("small_loaded")
        gathered = [[sem(f"gathered_{t}_{g}") for g in range(NG)] for t in range(TILES)]
        ident_zeroed = sem("ident_zeroed")
        ident_ready = sem("ident_ready")
        row_of_ready = sem("row_of_ready")
        gram_ps_zeroed = sem("gram_ps_zeroed")
        hi_ready = sem("hi_ready")
        lo_ready = sem("lo_ready")
        dense_placed = sem("dense_placed")
        w1_summed = sem("w1_summed")
        onehot_ready = sem("onehot_ready")
        onehot_used = sem("onehot_used")
        flip_done = sem("flip_done")
        job_drained = sem("job_drained")
        gram_done = sem("gram_done")
        gram_turned = sem("gram_turned")
        pairs_packed = sem("pairs_packed")
        pairs_turned = sem("pairs_turned")
        pairs_t_ready = sem("pairs_t_ready")
        h1_done = sem("h1_done")
        h1_low_ready = sem("h1_low_ready")
        h1_high_ready = sem("h1_high_ready")
        h2_done = sem("h2_done")
        h2_ready = sem("h2_ready")
        y_done = sem("y_done")
        y_ready = sem("y_ready")
        stored = sem("stored")

        def parts(f, *held):
            c, rest = full(f), tables[f].shape[0] % P
            yield P, tables[f][0:c * P, :].rearrange("(p c) d -> p c d", c=c), 0, *(h[:, 0:c, :] for h in held)
            if rest:
                yield rest, tables[f][c * P:c * P + rest, :], 1, *(h[0:rest, c, :] for h in held)

        def parts_before(n):
            return sum(len(list(parts(f))) for f in BY_PRODUCT[:n])

        def chunks_before(n):
            return sum(len(chunks(f)) for f in BY_PRODUCT[:n])

        block = ctx.enter_context(nc.Block())

        @block.sync
        def _(sp):
            sp.dma_start(index[:], ids.rearrange("(t p) f -> p t f", p=P)).then_inc(index_loaded, 16)
            for n, f in enumerate(BY_PRODUCT):
                if n >= IBUF:
                    sp.wait_ge(onehot_ready, chunks_before(n - IBUF + 1))
                sp.dma_start(id_row[:, n % IBUF, :], ids_t[f:f + 1, :].to_broadcast([P, B]))\
                  .then_inc(id_row_loaded[n], 16)
                if n >= TBUF:
                    sp.wait_ge(hi_ready, parts_before(n - TBUF + 1))
                    sp.wait_ge(lo_ready, parts_before(n - TBUF + 1))
                for r0, part, _, dst in parts(f, table[:, n % TBUF]):
                    sp.dma_start(dst, part).then_inc(table_loaded[n], 16)
            sp.wait_ge(y_ready, TILES)
            sp.dma_start(out.rearrange("b a -> a b"), y[:]).then_inc(stored, 16)
            sp.wait_ge(stored, 16)

        @block.gpsimd
        def _(pool):
            nc.gpsimd.memset(ident[:], 0.0).then_inc(ident_zeroed, 1)
            for s in SIZES:
                c = s // P
                nc.gpsimd.iota(row_of[s][:, 0:c], [[1, c]], base=0, channel_multiplier=c,
                               allow_small_or_imprecise_dtypes=True).then_inc(row_of_ready, 1)
                nc.gpsimd.iota(row_of[s][:, c:c + 1], [[0, 1]], base=c * P, channel_multiplier=1,
                               allow_small_or_imprecise_dtypes=True).then_inc(row_of_ready, 1)
            pool.wait_ge(ident_zeroed, 1)
            nc.gpsimd.affine_select(out=ident[:], in_=ident[:], compare_op=ALU.not_equal, fill=1.0, base=0,
                                    pattern=[[-1, P]], channel_multiplier=1).then_inc(ident_ready, 1)
            pool.wait_ge(index_loaded, 16)
            for t in range(TILES):
                for g, group in enumerate(GROUPS):
                    for i, f in enumerate(group):
                        nc.gpsimd.indirect_dma_start(
                            rows[:, t, g * GROUP + i, :], None, tables[f],
                            bass.IndirectOffsetOnAxis(index[:, t, f:f + 1], 0)).then_inc(gathered[t][g], 16)

        @block.vector
        def _(dve):
            dve.wait_ge(row_of_ready, 2 * len(SIZES))

            done = [0]

            def make_low_part(n, f):
                if n >= TBUF:
                    dve.wait_ge(onehot_used, chunks_before(n - TBUF + 1))
                for _, _, i, whole, hi, lo in parts(f, table[:, n % TBUF], table_hi[:, n % TBUF],
                                                    table_lo[:, n % TBUF]):
                    dve.wait_ge(hi_ready, parts_before(n) + i + 1)
                    nc.vector.tensor_tensor(lo, whole, hi.bitcast(fp32), ALU.subtract).then_inc(lo_ready, 1)

            def make_onehots(n, f):
                dve.wait_ge(id_row_loaded[n], 16)
                if n == 0:
                    make_low_part(n, f)
                for c, k in enumerate(chunks(f)):
                    if done[0] >= OBUF:
                        dve.wait_ge(onehot_used, done[0] - OBUF + 1)
                    nc.vector.tensor_scalar(onehot[0:k, done[0] % OBUF, :], id_row[0:k, n % IBUF, :],
                                            row_of[tables[f].shape[0]][0:k, c:c + 1], None,
                                            ALU.is_equal).then_inc(onehot_ready, 1)
                    done[0] += 1

            def pack_pairs(t):
                dve.wait_ge(gram_done, P // GQ * (t + 1))
                if t:
                    dve.wait_ge(pairs_packed, F * t)
                nc.vector.transpose(
                    gram_t[:].rearrange("p g (k i) -> p g k i", k=2),
                    gram_ps[:, t % GBUF, :, 0:HALF * F].rearrange("p k (i g) -> p g k i", g=F))\
                    .then_inc(gram_turned, 1)
                dve.wait_ge(gram_turned, t + 1)
                if t:
                    dve.wait_ge(pairs_turned, t)
                for g in range(F):
                    nc.vector.tensor_copy(pairs[:, PAIR0[g]:PAIR0[g] + F - g],
                                          gram_t[:, g, g:F]).then_inc(pairs_packed, 1)

            for kind, a, b in JOBS:
                if kind == "product":
                    make_onehots(a, BY_PRODUCT[a])
                    if a + 1 < len(BY_PRODUCT):
                        make_low_part(a + 1, BY_PRODUCT[a + 1])
                    if a == 0:
                        nc.vector.memset(gram_ps[:], 0.0).then_inc(gram_ps_zeroed, 1)
                        dve.wait_ge(w1d_loaded, 32)
                        nc.vector.tensor_tensor(w1s[:], w1d[:, 0, :], w1d[:, 1, :], ALU.add).then_inc(w1_summed, 1)
                elif kind == "gram" and b == P // GQ - 1:
                    pack_pairs(a)
                elif kind == "layer1":
                    dve.wait_ge(h1_done, 2 * a + 2)
                    if a:
                        dve.wait_ge(h2_done, a)
                    else:
                        dve.wait_ge(small_loaded, 48)
                    for m in range(H1B // 2, H1B):
                        o = (m - H1B // 2) * P
                        nc.vector.tensor_scalar(h1[:, m, :], z_ps[:, o:o + P], b1s[:, m:m + 1], 0.0,
                                                ALU.add, ALU.max).then_inc(h1_high_ready, 1)

        @block.scalar
        def _(act):
            act.dma_start(dense[:], dense_t).then_inc(dense_loaded, 16)
            act.dma_start(w1d[:, 0, :], w1[0:P, :]).then_inc(w1d_loaded, 16)
            act.dma_start(w1d[:, 1, :], w1[P + PAIRS:, :]).then_inc(w1d_loaded, 16)
            act.dma_start(w1p[:], w1[P:P + PAIRS, :].rearrange("(c p) n -> p c n", p=KP)).then_inc(w1p_loaded, 16)
            act.dma_start(w2s[:], w2.rearrange("(c p) n -> p c n", p=P)).then_inc(w2_loaded, 16)
            act.dma_start(b1s[:], b1_t).then_inc(small_loaded, 16)
            act.dma_start(b2s[:], b2_t).then_inc(small_loaded, 16)
            act.dma_start(w3s[:], w3_t).then_inc(small_loaded, 16)
            def make_high_part(n, f):
                act.wait_ge(table_loaded[n], 16 * len(list(parts(f))))
                if n >= TBUF:
                    act.wait_ge(onehot_used, chunks_before(n - TBUF + 1))
                for _, _, _, whole, hi in parts(f, table[:, n % TBUF], table_hi[:, n % TBUF]):
                    nc.scalar.activation(hi, whole, ACT.Copy).then_inc(hi_ready, 1)

            drained = 0
            make_high_part(0, BY_PRODUCT[0])
            act.wait_ge(dense_loaded, 16)
            nc.scalar.activation(et[:, :, 0], dense[:], ACT.Copy).then_inc(dense_placed, 1)
            for kind, a, b in JOBS:
                if kind == "product" and a + 1 < len(BY_PRODUCT):
                    make_high_part(a + 1, BY_PRODUCT[a + 1])
                if kind == "product":
                    act.wait_ge(onehot_used, chunks_before(a + 1))
                    nc.scalar.activation(et[:, :, BY_PRODUCT[a] + 1], job_ps[:, drained % JBUF, :],
                                         ACT.Copy).then_inc(job_drained, 1)
                    drained += 1
                elif kind == "flip":
                    act.wait_ge(flip_done, NG * a + b + 1)
                    found = runs(GROUPS[b])
                    for i, f, k in found:
                        copy = nc.scalar.activation(
                            et[:, a * P:(a + 1) * P, f + 1:f + 1 + k].rearrange("p b f -> p f b"),
                            job_ps[:, drained % JBUF, i * P:(i + k) * P].rearrange("p (f b) -> p f b", b=P),
                            ACT.Copy)
                    copy.then_inc(job_drained, 1)
                    drained += 1
                elif kind == "turn":
                    act.wait_ge(pairs_turned, a + 1)
                    if a:
                        act.wait_ge(h1_done, 2 * a)
                    nc.scalar.activation(pairs_t[:].rearrange("p c b -> p (c b)"), z_ps[0:KP, 0:KC * P],
                                         ACT.Copy).then_inc(pairs_t_ready, 1)
                elif kind == "layer1":
                    if a == 0:
                        act.wait_ge(small_loaded, 48)
                    else:
                        act.wait_ge(h2_done, a)
                    act.wait_ge(h1_done, 2 * a + 1)
                    for m in range(H1B // 2):
                        nc.scalar.activation(h1[:, m, :], h_ps[:, m * P:(m + 1) * P],
                                             ACT.Relu, bias=b1s[:, m:m + 1]).then_inc(h1_low_ready, 1)
                elif kind == "layer2":
                    act.wait_ge(h2_done, a + 1)
                    if a:
                        act.wait_ge(y_done, a)
                    for m in range(H2B):
                        nc.scalar.activation(h2[:, m, :], h_ps[:, m * P:(m + 1) * P], ACT.Relu,
                                             bias=b2s[:, m:m + 1]).then_inc(h2_ready, 1)
                elif kind == "layer3":
                    act.wait_ge(y_done, a + 1)
                    nc.scalar.activation(y[:, a * P:(a + 1) * P], z_ps[0:1, 0:P], ACT.Copy)\
                      .then_inc(y_ready, 1)

        @block.tensor
        def _(pe):
            pe.wait_ge(ident_ready, 1)
            jobs = 0
            for kind, a, b in JOBS:
                if kind in ("product", "flip"):
                    bank = jobs % JBUF
                    if jobs >= JBUF:
                        pe.wait_ge(job_drained, jobs - JBUF + 1)
                    jobs += 1
                if kind == "product":
                    pe.wait_ge(hi_ready, parts_before(a + 1))
                    pe.wait_ge(lo_ready, parts_before(a + 1))
                    sizes = chunks(BY_PRODUCT[a])
                    for c, k in enumerate(sizes):
                        used = chunks_before(a) + c
                        pe.wait_ge(onehot_ready, used + 1)
                        nc.tensor.matmul(job_ps[:, bank, :], table_hi[0:k, a % TBUF, c, :],
                                         onehot[0:k, used % OBUF, :], start=c == 0, stop=False)
                        nc.tensor.matmul(job_ps[:, bank, :], table_lo[0:k, a % TBUF, c, :],
                                         onehot[0:k, used % OBUF, :], start=False,
                                         stop=c == len(sizes) - 1).then_inc(onehot_used, 1)
                elif kind == "flip":
                    pe.wait_ge(gathered[a][b], 16 * len(GROUPS[b]))
                    for i in range(len(GROUPS[b])):
                        flip = nc.tensor.transpose(job_ps[:, bank, i * P:(i + 1) * P],
                                                   rows[:, a, b * GROUP + i, :], ident[:])
                    flip.then_inc(flip_done, 1)
                elif kind == "gram":
                    if b == 0:
                        pe.wait_ge(job_drained, column_jobs_for(a))
                        if a == 0:
                            pe.wait_ge(dense_placed, 1)
                            pe.wait_ge(gram_ps_zeroed, 1)
                        if a >= GBUF:
                            pe.wait_ge(gram_turned, a - GBUF + 1)
                    for i in range(GQ):
                        e = et[:, a * P + b * GQ + i, :]
                        o = (i % HALF) * F
                        gram = nc.tensor.matmul(gram_ps[b * GQ:b * GQ + F, a % GBUF, i // HALF, o:o + F],
                                                e[:, 1:N], e[:, 0:F], start=True, stop=True)
                    gram.then_inc(gram_done, 1)
                elif kind == "turn":
                    if a:
                        pe.wait_ge(y_ready, a)
                    for c in range(KC):
                        pe.wait_ge(pairs_packed, F * a + sum(PAIR0[g] < (c + 1) * KP for g in range(F)))
                        turn = nc.tensor.transpose(z_ps[0:KP, c * P:(c + 1) * P],
                                                   pairs[:, c * KP:(c + 1) * KP], ident[:])
                    turn.then_inc(pairs_turned, 1)
                elif kind == "layer1":
                    if a == 0:
                        pe.wait_ge(w1_summed, 1)
                        pe.wait_ge(dense_loaded, 16)
                        pe.wait_ge(w1p_loaded, 16)
                    else:
                        pe.wait_ge(h2_ready, H2B * a)
                    for m in range(H1B):
                        if m == H1B // 2:
                            pe.wait_ge(pairs_t_ready, a + 1)
                        o = (h_ps if m < H1B // 2 else z_ps)[:, (m % 2) * P:(m % 2 + 1) * P]
                        nc.tensor.matmul(o, w1s[:, m * P:(m + 1) * P], dense[:, a * P:(a + 1) * P],
                                         start=True, stop=False)
                        if m == 0:
                            pe.wait_ge(pairs_t_ready, a + 1)
                        for c in range(KC):
                            layer = nc.tensor.matmul(o, w1p[:, c, m * P:(m + 1) * P], pairs_t[:, c, :],
                                                     start=False, stop=c == KC - 1)
                        if m % 2:
                            layer.then_inc(h1_done, 1)
                elif kind == "layer2":
                    if a == 0:
                        pe.wait_ge(w2_loaded, 16)
                    for m in range(H2B):
                        for c in range(H1B):
                            if m == 0 and c == 0:
                                pe.wait_ge(h1_low_ready, H1B // 2 * (a + 1))
                            elif m == 0 and c >= H1B // 2:
                                pe.wait_ge(h1_high_ready, H1B // 2 * (a - 1) + c + 1)
                            layer = nc.tensor.matmul(h_ps[:, m * P:(m + 1) * P], w2s[:, c, m * P:(m + 1) * P],
                                                     h1[:, c, :], start=c == 0, stop=c == H1B - 1)
                    layer.then_inc(h2_done, 1)
                else:
                    pe.wait_ge(h2_ready, H2B * (a + 1))
                    if a == 0:
                        pe.wait_ge(small_loaded, 48)
                    for c in range(H2B):
                        layer = nc.tensor.matmul(z_ps[0:1, 0:P], w3s[:, c:c + 1], h2[:, c, :],
                                                 start=c == 0, stop=c == H2B - 1)
                    layer.then_inc(y_done, 1)


def kernel(**inputs):
    import numpy as np
    import concourse.bacc as bacc
    from concourse.bass_utils import run_bass_kernel_spmd

    def columns(v):
        return v.reshape(-1, 128).T

    given = {
        "dense_t": np.asarray(inputs["r_dense_features"]).T,
        "ids": np.asarray(inputs["ids"]),
        "ids_t": np.asarray(inputs["ids"]).T,
        **{f"tbl_{f}": np.asarray(inputs[f"tbl_{f}"]) for f in range(26)},
        "w1": np.asarray(inputs["W_top1"]),
        "b1_t": columns(np.asarray(inputs["b_top1"])),
        "w2": np.asarray(inputs["W_top2"]),
        "b2_t": columns(np.asarray(inputs["b_top2"])),
        "w3_t": columns(np.asarray(inputs["W_top3"])),
    }
    nc = bacc.Bacc("TRN2", target_bir_lowering=False, num_devices=1)
    arrays, aps = {}, {}
    for name, array in given.items():
        arrays[name] = np.ascontiguousarray(array)
        aps[name] = nc.dram_tensor(name, arrays[name].shape, mybir.dt.from_np(arrays[name].dtype),
                                   kind="ExternalInput").ap()
    out = nc.dram_tensor("out", (512, 1), mybir.dt.float32, kind="ExternalOutput").ap()
    dlrm_tower(nc, aps["dense_t"], aps["ids"], aps["ids_t"], [aps[f"tbl_{f}"] for f in range(26)],
               aps["w1"], aps["b1_t"], aps["w2"], aps["b2_t"], aps["w3_t"], out)
    return run_bass_kernel_spmd(nc, [arrays], core_ids=[0]).results[0]["out"]
```

```python
import concourse.bass as bass
from concourse import mybir
from contextlib import ExitStack


def dlrm_tower(nc, dense_t, ids, ids_t, tables, w1, b1_t, w2, b2_t, w3_t, out):
    fp32 = mybir.dt.float32
    fp32r = mybir.dt.float32r
    i32 = mybir.dt.int32
    ALU = mybir.AluOpType
    ACT = mybir.ActivationFunctionType

    P = 128
    D, B = dense_t.shape
    F = len(tables)
    N = F + 1
    BLOCK = 32
    SLOT = 28
    TILES = B // P
    H1, H2 = w2.shape
    H1B, H2B = H1 // P, H2 // P
    PAIRS = N * (N - 1) // 2
    KC = 3
    PAIR0 = [g * (N - 1) - g * (g - 1) // 2 for g in range(N)]
    RECTS = [(g, min(g + 3, N - 1)) for g in range(0, N - 1, 3)]
    RECT0 = [sum((g1 - g0) * (N - 1 - g0) for g0, g1 in RECTS[:k]) for k in range(len(RECTS) + 1)]
    assert RECT0[-1] <= KC * P
    SHARE = 4
    HALF = BLOCK // 2

    BY_PRODUCT = [0, 12, 13, 22, 23, 24, 25, 11, 10]
    assert all(tables[f].shape[0] <= 10 * P and tables[f].shape[0] % P for f in BY_PRODUCT)
    GATHERED = [f for f in range(F) if f not in BY_PRODUCT]
    GROUP = 4
    GROUPS = [GATHERED[i:i + GROUP] for i in range(0, len(GATHERED), GROUP)]
    NG = len(GROUPS)

    def full(f):
        return tables[f].shape[0] // P

    def chunks(f):
        return [P] * full(f) + [tables[f].shape[0] % P]

    MAXC = max(len(chunks(f)) for f in BY_PRODUCT)
    SIZES = sorted({tables[f].shape[0] for f in BY_PRODUCT})
    WARM_UP = 16
    HEAD = 2
    PARTS = 3
    RBUF = 3
    TBUF = 2
    IBUF = 4
    OBUF = 8
    JBUF = 2
    GBUF = 2

    BLOCKS = P // BLOCK
    QUARTERS = 4
    ORDER = """
        product 0, product 1, flip 0.0, product 2, product 3, flip 0.1, flip 0.2, product 4,
        product 5, flip 0.3, flip 0.4, product 6, flip 1.0, flip 1.1, product 7, flip 1.2,
        flip 1.3, product 8, gram 0.0, gram 0.1, flip 1.4, gram 0.2, gram 0.3, gram 1.0, flip 2.0,
        gram 1.1, gram 1.2, flip 2.1, flip 2.2, turn 0, gram 1.3, layer1 0.0, layer1 0.1, flip 2.3,
        flip 2.4, layer2 0, gram 2.0, turn 1, layer3 0, flip 3.0, layer1 1.0, gram 2.1, layer1 1.1,
        gram 2.2, gram 2.3, layer2 1, flip 3.1, turn 2, layer3 1, flip 3.2, layer1 2.0, flip 3.3,
        flip 3.4, layer1 2.1, gram 3.0, gram 3.1, gram 3.2, gram 3.3, layer2 2, turn 3, layer3 2,
        layer1 3.0, layer1 3.1, layer2 3, layer3 3
    """
    JOBS = []
    for job in ORDER.split(","):
        kind, place = job.split()
        tile, _, part = place.partition(".")
        JOBS.append((kind, int(tile), int(part) if part else None))

    def runs(group):
        found = []
        for i, f in enumerate(group):
            if found and found[-1][1] + found[-1][2] == f:
                found[-1][2] += 1
            else:
                found.append([i, f, 1])
        return found

    with ExitStack() as ctx:
        def sb(name, shape, dt=fp32):
            return ctx.enter_context(nc.sbuf_tensor(name, shape, dt))

        def ps(name, shape):
            return ctx.enter_context(nc.psum_tensor(name, shape, fp32))

        def sem(name):
            return ctx.enter_context(nc.semaphore(name))

        index = sb("index", [P, TILES, F], i32)
        id_row = sb("id_row", [P, IBUF, B], i32)
        row = sb("row", [P, len(SIZES), 2])
        minus_row = sb("minus_row", [P, len(SIZES), 2])
        table = sb("table", [P, RBUF, MAXC, D])
        table_hi = sb("table_hi", [P, TBUF, MAXC, D], fp32r)
        table_lo = sb("table_lo", [P, TBUF, MAXC, D], fp32r)
        offset = sb("offset", [P, IBUF, B])
        onehot = sb("onehot", [P, OBUF, B], fp32r)
        gap = sb("gap", [P, B])
        last_onehot = sb("last_onehot", [P, TBUF, B], fp32r)
        rows = sb("rows", [P, TILES, len(GATHERED), D])
        et = sb("et", [P, B, SLOT])
        dense = sb("dense", [P, B])
        ident = sb("ident", [P, P])
        w1d = sb("w1d", [P, 2, H1])
        w1s = sb("w1s", [P, H1])
        w1p = sb("w1p", [P, KC, H1])
        w2s = sb("w2s", [P, H1B, H2])
        w3s = sb("w3s", [P, H2B])
        b1s = sb("b1s", [P, H1B])
        b2s = sb("b2s", [P, H2B])
        gram_t = sb("gram_t", [P, F, BLOCK])
        pairs = sb("pairs", [P, KC * P])
        pairs_t = sb("pairs_t", [P, KC, P])
        h1 = sb("h1", [P, H1B, P])
        h2 = sb("h2", [P, H2B, P])
        y = sb("y", [1, B])

        flip_ps = ps("flip_ps", [P, JBUF, 512])
        gram_ps = ps("gram_ps", [P, GBUF, 2, 512])
        z_ps = ps("z_ps", [P, 512])
        h_ps = ps("h_ps", [P, 512])

        index_loaded = sem("index_loaded")
        id_row_loaded = [sem(f"id_row_loaded_{n}") for n in range(len(BY_PRODUCT))]
        table_loaded = [[sem(f"table_loaded_{n}_{i}") for i in range(PARTS)] for n in range(len(BY_PRODUCT))]
        dense_loaded = sem("dense_loaded")
        w1d_loaded = sem("w1d_loaded")
        w1p_zeroed = sem("w1p_zeroed")
        w1p_loaded = sem("w1p_loaded")
        w2_loaded = sem("w2_loaded")
        small_loaded = sem("small_loaded")
        gathered = [[sem(f"gathered_{t}_{g}") for g in range(NG)] for t in range(TILES)]
        pairs_padded = sem("pairs_padded")
        ident_zeroed = sem("ident_zeroed")
        ident_ready = sem("ident_ready")
        row_ready = sem("row_ready")
        minus_row_ready = sem("minus_row_ready")
        gram_ps_zeroed = sem("gram_ps_zeroed")
        hi_ready = sem("hi_ready")
        lo_ready = sem("lo_ready")
        dense_placed = sem("dense_placed")
        w1_summed = sem("w1_summed")
        first_offset_ready = sem("first_offset_ready")
        offset_ready = sem("offset_ready")
        gap_ready = sem("gap_ready")
        onehot_ready = sem("onehot_ready")
        last_onehot_ready = sem("last_onehot_ready")
        onehot_used = sem("onehot_used")
        flip_done = sem("flip_done")
        product_drained = sem("product_drained")
        flip_drained = sem("flip_drained")
        gram_done = sem("gram_done")
        gram_turned = sem("gram_turned")
        pairs_low_packed = sem("pairs_low_packed")
        pairs_high_packed = sem("pairs_high_packed")
        pairs_turned = sem("pairs_turned")
        pairs_t_ready = sem("pairs_t_ready")
        h1_done = sem("h1_done")
        h1_low_ready = sem("h1_low_ready")
        h1_high_ready = sem("h1_high_ready")
        h2_done = sem("h2_done")
        h2_low_ready = sem("h2_low_ready")
        h2_high_ready = sem("h2_high_ready")
        y_done = sem("y_done")
        y_ready = sem("y_ready")
        stored = sem("stored")

        def parts(f, *held):
            c = full(f)
            whole = tables[f][0:c * P, :].rearrange("(p c) d -> p c d", c=c)
            for c0, c1 in ((0, HEAD), (HEAD, c)):
                yield whole[:, c0:c1, :], *(h[:, c0:c1, :] for h in held)
            yield tables[f][c * P:, :], *(h[0:tables[f].shape[0] % P, c, :] for h in held)

        def weight_runs():
            for k, (g0, g1) in enumerate(RECTS):
                for g in range(g0, g1):
                    first, to, left = P + PAIR0[g], RECT0[k] + (g - g0) * (N - 1 - g0) + g - g0, N - 1 - g
                    while left:
                        count = min(left, P - to % P)
                        yield first, to, count
                        first, to, left = first + count, to + count, left - count

        def rectangle(k):
            g0, g1 = RECTS[k]
            return (pairs[:, RECT0[k]:RECT0[k + 1]].rearrange("p (g r) -> p g r", g=g1 - g0), gram_t[:, g0:g1, g0:F])

        def turn_ps(t):
            return z_ps[:] if t < TILES - 1 else gram_ps[:, (t + 1) % GBUF, 0]

        def y_ps(t):
            return flip_ps[0:1, 0, 0:P] if t == TILES - 2 else h_ps[0:1, 0:P]

        def size_of(f):
            return SIZES.index(tables[f].shape[0])

        def parts_before(n):
            return PARTS * n

        def full_before(n):
            return sum(full(f) for f in BY_PRODUCT[:n])

        def uses_before_full(k):
            return k + sum(k > full_before(n + 1) for n in range(len(BY_PRODUCT)))

        def chunks_before(n):
            return sum(len(chunks(f)) for f in BY_PRODUCT[:n])

        block = ctx.enter_context(nc.Block())

        @block.sync
        def _(sp):
            sp.dma_start(index[:], ids.rearrange("(t p) f -> p t f", p=P)).then_inc(index_loaded, 16)
            for n, f in enumerate(BY_PRODUCT):
                if n >= IBUF:
                    if n > IBUF:
                        sp.wait_ge(offset_ready, n - IBUF)
                    else:
                        sp.wait_ge(first_offset_ready, 1)
                    sp.wait_ge(last_onehot_ready, n - IBUF + 1)
                sp.dma_start(id_row[:, n % IBUF, :], ids_t[f:f + 1, :].to_broadcast([P, B]))\
                  .then_inc(id_row_loaded[n], 16)
                if n >= RBUF:
                    sp.wait_ge(hi_ready, parts_before(n - RBUF + 1))
                    sp.wait_ge(lo_ready, parts_before(n - RBUF + 1))
                for i, (part, dst) in enumerate(parts(f, table[:, n % RBUF])):
                    sp.dma_start(dst, part).then_inc(table_loaded[n][i], 16)
                if n == 3:
                    sp.dma_start(dense[:], dense_t).then_inc(dense_loaded, 16)
            sp.dma_start(w1d[:, 0, :], w1[0:P, :]).then_inc(w1d_loaded, 16)
            sp.dma_start(w1d[:, 1, :], w1[P + PAIRS:, :]).then_inc(w1d_loaded, 16)
            sp.wait_ge(w1p_zeroed, 1)
            for first, to, count in weight_runs():
                sp.dma_start(w1p[to % P:to % P + count, to // P, :], w1[first:first + count, :])\
                  .then_inc(w1p_loaded, 16)
            sp.dma_start(w2s[:], w2.rearrange("(c p) n -> p c n", p=P)).then_inc(w2_loaded, 16)
            sp.dma_start(b1s[:], b1_t).then_inc(small_loaded, 16)
            sp.dma_start(b2s[:], b2_t).then_inc(small_loaded, 16)
            sp.dma_start(w3s[:], w3_t).then_inc(small_loaded, 16)
            sp.wait_ge(y_ready, TILES)
            sp.dma_start(out.rearrange("b a -> a b"), y[:]).then_inc(stored, 16)
            sp.wait_ge(stored, 16)

        @block.gpsimd
        def _(pool):
            nc.gpsimd.memset(ident[:], 0.0).then_inc(ident_zeroed, 1)
            pool.wait_ge(ident_zeroed, 1)
            nc.gpsimd.affine_select(out=ident[:], in_=ident[:], compare_op=ALU.not_equal, fill=1.0, base=0,
                                    pattern=[[-1, P]], channel_multiplier=1).then_inc(ident_ready, 1)
            for i, s in enumerate(SIZES):
                nc.gpsimd.iota(row[:, i, 0:1], [[0, 1]], base=0, channel_multiplier=s // P,
                               allow_small_or_imprecise_dtypes=True).then_inc(row_ready, 1)
                nc.gpsimd.iota(row[:, i, 1:2], [[0, 1]], base=s // P * P, channel_multiplier=1,
                               allow_small_or_imprecise_dtypes=True).then_inc(row_ready, 1)
            pool.wait_ge(index_loaded, 16)
            for t in range(TILES):
                for g, group in enumerate(GROUPS):
                    for i, f in enumerate(group):
                        nc.gpsimd.indirect_dma_start(
                            rows[:, t, g * GROUP + i, :], None, tables[f],
                            bass.IndirectOffsetOnAxis(index[:, t, f:f + 1], 0)).then_inc(gathered[t][g], 16)

        @block.vector
        def _(dve):
            nc.vector.memset(w1p[:], 0.0).then_inc(w1p_zeroed, 1)
            nc.vector.memset(pairs[:, RECT0[-1]:], 0.0).then_inc(pairs_padded, 1)

            dve.wait_ge(minus_row_ready, 1)
            dve.wait_ge(id_row_loaded[0], 16)
            nc.vector.tensor_scalar(offset[:, 0, :], id_row[:, 0, :], minus_row[:, size_of(BY_PRODUCT[0]), 0:1],
                                    None, ALU.add).then_inc(first_offset_ready, 1)

            def make_low_parts(n, f, i0, i1):
                if i0 == 0 and n >= TBUF:
                    dve.wait_ge(onehot_used, chunks_before(n - TBUF + 1))
                split = list(parts(f, table[:, n % RBUF], table_hi[:, n % TBUF], table_lo[:, n % TBUF]))
                for i, (_, whole, hi, lo) in enumerate(split[i0:i1], i0):
                    dve.wait_ge(hi_ready, parts_before(n) + i + 1)
                    nc.vector.tensor_tensor(lo, whole, hi.bitcast(fp32), ALU.subtract).then_inc(lo_ready, 1)

            def make_onehots(n, f, c0, c1):
                if n == 0:
                    dve.wait_ge(first_offset_ready, 1)
                else:
                    dve.wait_ge(offset_ready, n)
                for c in range(c0, c1):
                    done = full_before(n) + c
                    if done >= OBUF:
                        dve.wait_ge(onehot_used, uses_before_full(done - OBUF + 1))
                    nc.vector.tensor_scalar(onehot[:, done % OBUF, :], offset[:, n % IBUF, :],
                                            float(c), None, ALU.is_equal).then_inc(onehot_ready, 1)

            def turn_grams(t):
                dve.wait_ge(gram_done, QUARTERS * (t + 1))
                grams = gram_ps[:, t % GBUF, :, 0:HALF * F].rearrange("p k (i g) -> p g k i", g=F)
                for g0, g1, read, count in ((0, RECTS[SHARE][0], pairs_low_packed, SHARE),
                                            (RECTS[SHARE][0], F, pairs_high_packed, len(RECTS) - SHARE)):
                    if t:
                        dve.wait_ge(read, count * t)
                    nc.vector.transpose(gram_t[:, g0:g1, :].rearrange("p g (k i) -> p g k i", k=2),
                                        grams[:, g0:g1]).then_inc(gram_turned, 1)

            for kind, a, b in JOBS:
                if kind == "product":
                    f = BY_PRODUCT[a]
                    make_onehots(a, f, 0, HEAD)
                    make_low_parts(a, f, 0, 1)
                    make_onehots(a, f, HEAD, 2 * HEAD)
                    make_low_parts(a, f, 1, PARTS)
                    make_onehots(a, f, 2 * HEAD, full(f))
                    if a == len(BY_PRODUCT) - 1:
                        nc.vector.memset(gram_ps[:], 0.0).then_inc(gram_ps_zeroed, 1)
                        dve.wait_ge(w1d_loaded, 32)
                        nc.vector.tensor_tensor(w1s[:], w1d[:, 0, :], w1d[:, 1, :], ALU.add).then_inc(w1_summed, 1)
                elif kind == "gram" and b == QUARTERS - 1:
                    turn_grams(a)
                    dve.wait_ge(gram_turned, 2 * (a + 1))
                    if a:
                        dve.wait_ge(pairs_turned, a)
                    for k in range(SHARE, len(RECTS)):
                        nc.vector.tensor_copy(*rectangle(k)).then_inc(pairs_high_packed, 1)
                elif kind == "layer1" and b == 1:
                    dve.wait_ge(h1_done, 2 * a + 2)
                    if a:
                        dve.wait_ge(h2_done, 2 * a)
                    else:
                        dve.wait_ge(small_loaded, 48)
                    for m in range(H1B // 2, H1B):
                        o = (m - H1B // 2) * P
                        nc.vector.tensor_scalar(h1[:, m, :], z_ps[:, o:o + P], b1s[:, m:m + 1], 0.0,
                                                ALU.add, ALU.max).then_inc(h1_high_ready, 1)
                elif kind == "layer2":
                    dve.wait_ge(h2_done, 2 * a + 2)
                    if a:
                        dve.wait_ge(y_done, a)
                    nc.vector.tensor_scalar(h2[:, 1, :], z_ps[:, 0:P], b2s[:, 1:2], 0.0,
                                            ALU.add, ALU.max).then_inc(h2_high_ready, 1)

        @block.scalar
        def _(act):
            def make_high_part(n, f):
                if n >= TBUF:
                    act.wait_ge(onehot_used, chunks_before(n - TBUF + 1))
                for i, (_, whole, hi) in enumerate(parts(f, table[:, n % RBUF], table_hi[:, n % TBUF])):
                    act.wait_ge(table_loaded[n][i], 16)
                    nc.scalar.activation(hi, whole, ACT.Copy).then_inc(hi_ready, 1)

            def make_offset(n, f):
                act.wait_ge(id_row_loaded[n], 16)
                if n >= IBUF:
                    act.wait_ge(onehot_ready, full_before(n - IBUF + 1))
                nc.scalar.activation(offset[:, n % IBUF, :], id_row[:, n % IBUF, :], ACT.Identity,
                                     bias=minus_row[:, size_of(f), 0:1]).then_inc(offset_ready, 1)

            def make_last_onehot(n, f):
                k = tables[f].shape[0] % P
                if n:
                    act.wait_ge(last_onehot_ready, n)
                nc.scalar.activation(gap[0:k, :], id_row[0:k, n % IBUF, :], ACT.Abs,
                                     bias=minus_row[0:k, size_of(f), 1:2]).then_inc(gap_ready, 1)
                act.wait_ge(gap_ready, n + 1)
                if n >= TBUF:
                    act.wait_ge(onehot_used, chunks_before(n - TBUF + 1))
                nc.scalar.activation(last_onehot[0:k, n % TBUF, :], gap[0:k, :], ACT.Relu, scale=-1.0,
                                     bias=1.0).then_inc(last_onehot_ready, 1)

            act.wait_ge(row_ready, 2 * len(SIZES))
            nc.scalar.activation(minus_row[:], row[:], ACT.Copy, scale=-1.0).then_inc(minus_row_ready, 1)
            act.wait_ge(minus_row_ready, 1)
            make_high_part(0, BY_PRODUCT[0])
            make_last_onehot(0, BY_PRODUCT[0])
            make_offset(1, BY_PRODUCT[1])
            for kind, a, b in JOBS:
                if kind == "product" and a + 1 < len(BY_PRODUCT):
                    make_high_part(a + 1, BY_PRODUCT[a + 1])
                    make_last_onehot(a + 1, BY_PRODUCT[a + 1])
                    if a + 2 < len(BY_PRODUCT):
                        make_offset(a + 2, BY_PRODUCT[a + 2])
                elif kind == "product":
                    act.wait_ge(dense_loaded, 16)
                    nc.scalar.activation(et[:, :, 0], dense[:], ACT.Copy).then_inc(dense_placed, 1)
                if kind == "product":
                    act.wait_ge(onehot_used, chunks_before(a + 1))
                    cuts = (0, P, B) if a == len(BY_PRODUCT) - 1 else (0, B)
                    for b0, b1 in zip(cuts, cuts[1:]):
                        nc.scalar.activation(et[:, b0:b1, BY_PRODUCT[a] + 1], (h_ps, z_ps)[a % 2][:, b0:b1],
                                             ACT.Copy).then_inc(product_drained, 1)
                elif kind == "flip":
                    act.wait_ge(flip_done, NG * a + b + 1)
                    found = runs(GROUPS[b])
                    for i, f, k in found:
                        copy = nc.scalar.activation(
                            et[:, a * P:(a + 1) * P, f + 1:f + 1 + k].rearrange("p b f -> p f b"),
                            flip_ps[:, (NG * a + b) % JBUF, i * P:(i + k) * P].rearrange("p (f b) -> p f b", b=P),
                            ACT.Copy)
                    copy.then_inc(flip_drained, 1)
                elif kind == "gram" and b == QUARTERS - 1:
                    act.wait_ge(gram_turned, 2 * a + 1)
                    if a:
                        act.wait_ge(pairs_turned, a)
                    for k in range(SHARE):
                        nc.scalar.activation(*rectangle(k), ACT.Copy).then_inc(pairs_low_packed, 1)
                elif kind == "turn":
                    act.wait_ge(pairs_turned, a + 1)
                    if a:
                        act.wait_ge(h1_done, 2 * a)
                    nc.scalar.activation(pairs_t[:].rearrange("p c b -> p (c b)"), turn_ps(a)[:, 0:KC * P],
                                         ACT.Copy).then_inc(pairs_t_ready, 1)
                elif kind == "layer1" and b == 0:
                    if a == 0:
                        act.wait_ge(small_loaded, 48)
                    else:
                        act.wait_ge(h2_done, 2 * a)
                    act.wait_ge(h1_done, 2 * a + 1)
                    for m in range(H1B // 2):
                        nc.scalar.activation(h1[:, m, :], h_ps[:, m * P:(m + 1) * P],
                                             ACT.Relu, bias=b1s[:, m:m + 1]).then_inc(h1_low_ready, 1)
                elif kind == "layer2":
                    act.wait_ge(h2_done, 2 * a + 1)
                    if a:
                        act.wait_ge(y_done, a)
                    nc.scalar.activation(h2[:, 0, :], h_ps[:, 0:P], ACT.Relu,
                                         bias=b2s[:, 0:1]).then_inc(h2_low_ready, 1)
                elif kind == "layer3":
                    act.wait_ge(y_done, a + 1)
                    nc.scalar.activation(y[:, a * P:(a + 1) * P], y_ps(a), ACT.Copy)\
                      .then_inc(y_ready, 1)

        @block.tensor
        def _(pe):
            pe.wait_ge(ident_ready, 1)
            for _ in range(WARM_UP):
                nc.tensor.transpose(flip_ps[:, 0, 0:P], ident[:], ident[:])
            for kind, a, b in JOBS:
                if kind == "product":
                    if a >= 2:
                        pe.wait_ge(product_drained, a - 1)
                    product_ps = (h_ps, z_ps)[a % 2]
                    f = BY_PRODUCT[a]
                    for c, k in enumerate(chunks(f)):
                        part = parts_before(a) + (0, HEAD, full(f)).index(c) + 1 if c in (0, HEAD, full(f)) else 0
                        if part:
                            pe.wait_ge(hi_ready, part)
                        if c < full(f):
                            pe.wait_ge(onehot_ready, full_before(a) + c + 1)
                            hot = onehot[:, (full_before(a) + c) % OBUF, :]
                        else:
                            pe.wait_ge(last_onehot_ready, a + 1)
                            hot = last_onehot[0:k, a % TBUF, :]
                        nc.tensor.matmul(product_ps[:, :], table_hi[0:k, a % TBUF, c, :], hot,
                                         start=c == 0, stop=False)
                        if part:
                            pe.wait_ge(lo_ready, part)
                        nc.tensor.matmul(product_ps[:, :], table_lo[0:k, a % TBUF, c, :], hot,
                                         start=False, stop=c == full(f)).then_inc(onehot_used, 1)
                elif kind == "flip":
                    n = NG * a + b
                    if n >= JBUF:
                        pe.wait_ge(flip_drained, n - JBUF + 1)
                    pe.wait_ge(gathered[a][b], 16 * len(GROUPS[b]))
                    for i in range(len(GROUPS[b])):
                        flip = nc.tensor.transpose(flip_ps[:, n % JBUF, i * P:(i + 1) * P],
                                                   rows[:, a, b * GROUP + i, :], ident[:])
                    flip.then_inc(flip_done, 1)
                elif kind == "gram":
                    if b == 0:
                        pe.wait_ge(flip_drained, NG * (a + 1))
                        if a == 0:
                            pe.wait_ge(product_drained, len(BY_PRODUCT))
                            pe.wait_ge(dense_placed, 1)
                            pe.wait_ge(gram_ps_zeroed, 1)
                        if a == 1:
                            pe.wait_ge(product_drained, len(BY_PRODUCT) + 1)
                        if a >= GBUF:
                            pe.wait_ge(gram_turned, 2 * (a - GBUF + 1))
                    for i in range(b * BLOCK // QUARTERS, (b + 1) * BLOCK // QUARTERS):
                        o = (i % HALF) * F
                        for j in range(BLOCKS):
                            e = et[:, a * P + j * BLOCK + i, :]
                            gram = nc.tensor.matmul(gram_ps[j * BLOCK:j * BLOCK + F, a % GBUF, i // HALF, o:o + F],
                                                    e[:, 1:N], e[:, 0:F], start=True, stop=True)
                    gram.then_inc(gram_done, 1)
                elif kind == "turn":
                    if 0 < a < TILES - 1:
                        pe.wait_ge(h2_high_ready, a)
                    elif a:
                        pe.wait_ge(gram_turned, 2 * a)
                    if a == 0:
                        pe.wait_ge(pairs_padded, 1)
                    for c in range(KC):
                        packed = sum(first < (c + 1) * P for first in RECT0[:-1])
                        if packed <= SHARE:
                            pe.wait_ge(pairs_low_packed, SHARE * a + packed)
                        else:
                            pe.wait_ge(pairs_low_packed, SHARE * (a + 1))
                            pe.wait_ge(pairs_high_packed, (len(RECTS) - SHARE) * a + packed - SHARE)
                        turn = nc.tensor.transpose(turn_ps(a)[:, c * P:(c + 1) * P], pairs[:, c * P:(c + 1) * P], ident[:])
                    turn.then_inc(pairs_turned, 1)
                elif kind == "layer1":
                    if a == 0 and b == 0:
                        pe.wait_ge(w1_summed, 1)
                        pe.wait_ge(dense_loaded, 16)
                        pe.wait_ge(w1p_loaded, 16 * len(list(weight_runs())))
                    elif b == 0:
                        if a < TILES - 1:
                            pe.wait_ge(y_ready, a)
                    else:
                        if a:
                            pe.wait_ge(h2_high_ready, a)
                        pe.wait_ge(pairs_t_ready, a + 1)
                    for i in range(H1B // 2):
                        m = H1B // 2 * b + i
                        o = (h_ps, z_ps)[b][:, i * P:(i + 1) * P]
                        nc.tensor.matmul(o, w1s[:, m * P:(m + 1) * P], dense[:, a * P:(a + 1) * P],
                                         start=True, stop=False)
                        if m == 0:
                            pe.wait_ge(pairs_t_ready, a + 1)
                        for c in range(KC):
                            layer = nc.tensor.matmul(o, w1p[:, c, m * P:(m + 1) * P], pairs_t[:, c, :],
                                                     start=False, stop=c == KC - 1)
                    layer.then_inc(h1_done, 1)
                elif kind == "layer2":
                    if a == 0:
                        pe.wait_ge(w2_loaded, 16)
                    for m in range(H2B):
                        for c in range(H1B):
                            if m == 0 and c == 0:
                                pe.wait_ge(h1_low_ready, H1B // 2 * (a + 1))
                            elif m == 0 and c >= H1B // 2:
                                pe.wait_ge(h1_high_ready, H1B // 2 * (a - 1) + c + 1)
                            layer = nc.tensor.matmul((h_ps, z_ps)[m][:, 0:P], w2s[:, c, m * P:(m + 1) * P],
                                                     h1[:, c, :], start=c == 0, stop=c == H1B - 1)
                        layer.then_inc(h2_done, 1)
                else:
                    if a == TILES - 2:
                        pe.wait_ge(flip_drained, NG * TILES)
                    pe.wait_ge(h2_low_ready, a + 1)
                    if a == 0:
                        pe.wait_ge(small_loaded, 48)
                    for c in range(H2B):
                        if c:
                            pe.wait_ge(h2_high_ready, a + 1)
                        layer = nc.tensor.matmul(y_ps(a), w3s[:, c:c + 1], h2[:, c, :],
                                                 start=c == 0, stop=c == H2B - 1)
                    layer.then_inc(y_done, 1)


def kernel(**inputs):
    import numpy as np
    import concourse.bacc as bacc
    from concourse.bass_utils import run_bass_kernel_spmd

    def columns(v):
        return v.reshape(-1, 128).T

    given = {
        "dense_t": np.asarray(inputs["r_dense_features"]).T,
        "ids": np.asarray(inputs["ids"]),
        "ids_t": np.asarray(inputs["ids"]).T,
        **{f"tbl_{f}": np.asarray(inputs[f"tbl_{f}"]) for f in range(26)},
        "w1": np.asarray(inputs["W_top1"]),
        "b1_t": columns(np.asarray(inputs["b_top1"])),
        "w2": np.asarray(inputs["W_top2"]),
        "b2_t": columns(np.asarray(inputs["b_top2"])),
        "w3_t": columns(np.asarray(inputs["W_top3"])),
    }
    nc = bacc.Bacc("TRN2", target_bir_lowering=False, num_devices=1)
    arrays, aps = {}, {}
    for name, array in given.items():
        arrays[name] = np.ascontiguousarray(array)
        aps[name] = nc.dram_tensor(name, arrays[name].shape, mybir.dt.from_np(arrays[name].dtype),
                                   kind="ExternalInput").ap()
    out = nc.dram_tensor("out", (512, 1), mybir.dt.float32, kind="ExternalOutput").ap()
    dlrm_tower(nc, aps["dense_t"], aps["ids"], aps["ids_t"], [aps[f"tbl_{f}"] for f in range(26)],
               aps["w1"], aps["b1_t"], aps["w2"], aps["b2_t"], aps["w3_t"], out)
    return run_bass_kernel_spmd(nc, [arrays], core_ids=[0]).results[0]["out"]
```
